# Optimizing a Trainium2 kernel written in Bass

```python
import numpy as np
import jax
import jax.numpy as jnp

def _softmax(x, axis=-1):
    return jax.nn.softmax(x, axis=axis)

def _gelu(x):
    return jax.nn.gelu(x, approximate=True)

def _silu(x):
    return jax.nn.silu(x)

def _sigmoid(x):
    return jax.nn.sigmoid(x)

def _layernorm(x, axis=-1, eps=1e-05):
    m = jnp.mean(x, axis=axis, keepdims=True)
    v = jnp.var(x, axis=axis, keepdims=True)
    return (x - m) / jnp.sqrt(v + eps)

def _scatter_add(tgt, idx, src, axis=0):
    return tgt.at[idx].add(src)

def _segment_sum(src, seg, n):
    return jax.ops.segment_sum(src, seg, n)
kernel_name = 'mk_rec_standalone_d1_rec_r8_704400'

def setup_inputs(seed: int=0):
    np.random.seed(seed)
    _w = jnp.asarray

    def _rec_inputs():
        import jax
        import jax.numpy as jnp
        _rk = jax.random.key(seed)
        r_inputs = -0.00103678 + 1.00048 * jax.random.normal(jax.random.fold_in(_rk, 1), (512, 40, 16), jnp.float32)
        return r_inputs
    r_inputs = _rec_inputs()

    def _L0_rec_setup():
        import jax, jax.numpy as jnp
        import numpy as np
        B, M, D = (256, 40, 16)
        UNITS = [100, 100, 100]
        W_SCALE = 0.05
        key = jax.random.key(seed)
        ks = jax.random.split(key, 6)
        inputs = jax.random.normal(ks[0], (B, M, D), dtype=jnp.float32)
        W0 = jax.random.normal(ks[1], (M, M, UNITS[0]), dtype=jnp.float32) * W_SCALE
        W1 = jax.random.normal(ks[2], (M, UNITS[0], UNITS[1]), dtype=jnp.float32) * W_SCALE
        W2 = jax.random.normal(ks[3], (M, UNITS[1], UNITS[2]), dtype=jnp.float32) * W_SCALE
        b0 = jnp.zeros((UNITS[0],), dtype=jnp.float32)
        b1 = jnp.zeros((UNITS[1],), dtype=jnp.float32)
        b2 = jnp.zeros((UNITS[2],), dtype=jnp.float32)
        lin_w = jax.random.normal(ks[4], (sum(UNITS), 1), dtype=jnp.float32) * W_SCALE
        lin_b = jnp.zeros((1,), dtype=jnp.float32)
        return {'inputs': inputs, 'W0': W0, 'W1': W1, 'W2': W2, 'b0': b0, 'b1': b1, 'b2': b2, 'lin_w': lin_w, 'lin_b': lin_b}
    _L0_rec_all = _L0_rec_setup()
    _L0_rec_in = {k: v for k, v in _L0_rec_all.items() if k in ('W0', 'W1', 'W2', 'b0', 'b1', 'b2', 'lin_w', 'lin_b')}
    del _L0_rec_all
    return {'r_inputs': r_inputs, 'L0_rec_W0': _L0_rec_in['W0'], 'L0_rec_W1': _L0_rec_in['W1'], 'L0_rec_W2': _L0_rec_in['W2'], 'L0_rec_b0': _L0_rec_in['b0'], 'L0_rec_b1': _L0_rec_in['b1'], 'L0_rec_b2': _L0_rec_in['b2'], 'L0_rec_lin_w': _L0_rec_in['lin_w'], 'L0_rec_lin_b': _L0_rec_in['lin_b']}

def reference(r_inputs, L0_rec_W0, L0_rec_W1, L0_rec_W2, L0_rec_b0, L0_rec_b1, L0_rec_b2, L0_rec_lin_w, L0_rec_lin_b):
    import jax
    import jax.numpy as jnp

    def _L0_rec_ref(inputs, W0, W1, W2, b0, b1, b2, lin_w, lin_b):
        import jax, jax.numpy as jnp
        import numpy as np
        B, M, D = (256, 40, 16)
        UNITS = [100, 100, 100]
        W_SCALE = 0.05
        Ws = [W0, W1, W2]
        bs = [b0, b1, b2]
        base = inputs
        curr = base
        logit = []
        for Wk, bk in zip(Ws, bs):
            z = jnp.einsum('bid,bjd->bdij', base, curr)
            curr = jnp.einsum('bdij,ijh->bhd', z, Wk) + bk[None, :, None]
            logit.append(curr)
        pooled = jnp.sum(jnp.concatenate(logit, axis=1), axis=-1)
        out = pooled @ lin_w + lin_b
        return out
    y = _L0_rec_ref(r_inputs, L0_rec_W0, L0_rec_W1, L0_rec_W2, L0_rec_b0, L0_rec_b1, L0_rec_b2, L0_rec_lin_w, L0_rec_lin_b)
    return y

_drawn_inputs = setup_inputs


def setup_inputs(seed=0):
    import zlib

    import numpy as np

    out = dict(_drawn_inputs(seed))
    spreads = {'L0_rec_b0': (0.0, 0.1), 'L0_rec_b1': (0.0, 0.292), 'L0_rec_b2': (0.0, 0.294)}
    factors = {}
    for name, (base, spread) in spreads.items():
        noise = np.random.default_rng([zlib.crc32(name.encode()), seed]).standard_normal(out[name].shape)
        drawn = base * np.exp(spread * noise) if base else spread * noise
        out[name] = jnp.asarray(drawn.astype(out[name].dtype))
    for name, factor in factors.items():
        out[name] = (out[name] * factor).astype(out[name].dtype)
    return out
```

```python
from contextlib import ExitStack

import concourse.bass as bass
from concourse import mybir

B, M, D = 512, 40, 16
H = 100
F = M + 1
J = H + 1
T = 3
C = (F // 2 + 1) // T
K = T * F
U = D // 2
N = 2 * B
NCH = U * C
SLOTS = 2 * C
LAG = 7
BODY = 2 * C
GI = 5
NG = M // GI + 1
DA, DB = 48, 64
WA, WB = F + 2, F + 3 * (C - 1)


def build(nc, xa, xw, w0_pairs, w1x, w2t, v_init, head, lin_b, out):
    fp32, f32r = mybir.dt.float32, mybir.dt.float32r
    ALU, ACT = mybir.AluOpType, mybir.ActivationFunctionType

    with ExitStack() as ctx:
        def sb(name, shape, dt=fp32):
            return ctx.enter_context(nc.sbuf_tensor(name, shape, dt))

        def sem(name):
            return ctx.enter_context(nc.semaphore(name))

        z_high = sb("z_high", [128, SLOTS, N], f32r)
        z_low = sb("z_low", [128, SLOTS, N], f32r)
        xb_z = sb("xb_z", [128, C, N])
        x_a = sb("x_a", [128, 2, N])
        wc_high = sb("wc_high", [128, C * J], f32r)
        wc_low = sb("wc_low", [128, C * J], f32r)
        wq_high = sb("wq_high", [128, C * J], f32r)
        wq_low = sb("wq_low", [128, C * J], f32r)
        pair_sb = sb("pair_sb", [128, 2, C * J])
        w2_d = sb("w2_d", [112, F * J])
        w1_post = sb("w1_post", [112, F * J])
        v_sb = sb("v_sb", [J, DB])
        head_sb = sb("head_sb", [H, 2])
        linb_sb = sb("linb_sb", [1, 1])
        const_sb = sb("const_sb", [1, 1])
        ones = sb("ones", [J, 1])
        acc = sb("acc", [J, N])
        out_sb = sb("out_sb", [1, B])
        c1_sb = [w1_post[0:J, i * N:(i + 1) * N] for i in range(2)]
        prod = w1_post[0:J, 2 * N:3 * N]

        c1_ps = [ctx.enter_context(nc.psum_tensor(f"c1_ps{i}", [128, N], fp32)) for i in range(2)]
        q_ps = [ctx.enter_context(nc.psum_tensor(f"q_ps{i}", [128, N], fp32)) for i in range(2)]
        v_ps = q_ps[1][0:H, B:B + M]
        const_ps = q_ps[1][0:1, 0:1]
        d_ps = [t[:, h * B:(h + 1) * B] for t in (c1_ps[1], q_ps[0]) for h in range(2)]
        out_ps = c1_ps[0][0:1, 0:B]

        d1 = nc.dram_tensor("d1", [DA, WB * J], fp32, kind="Internal")
        d2 = nc.dram_tensor("d2", [DB, WA * J], fp32, kind="Internal")

        xb_loaded = [sem(f"xb_loaded{c}") for c in range(C)]
        xa_loaded = [sem(f"xa_loaded{i}") for i in range(2)]
        w0_loaded, w1_loaded, w2_loaded = sem("w0_loaded"), sem("w1_loaded"), sem("w2_loaded")
        small_loaded = sem("small_loaded")
        d_stored = sem("d_stored")
        dpair_loaded = sem("dpair_loaded")
        out_stored = sem("out_stored")
        v_done, v_copied = sem("v_done"), sem("v_copied")
        dgroup_done, dgroup_copied = sem("dgroup_done"), sem("dgroup_copied")
        wsum_done, wc_ready, wq_ready = sem("wsum_done"), sem("wc_ready"), sem("wq_ready")
        whigh_done = sem("whigh_done")
        filled, t2_cleared = sem("filled"), sem("t2_cleared")
        z_done, high_done, low_done = sem("z_done"), sem("high_done"), sem("low_done")
        c1_done, c1_psum_free, c1_copied = sem("c1_done"), sem("c1_psum_free"), sem("c1_copied")
        z_slots_free, q_psum_free = sem("z_slots_free"), sem("q_psum_free")
        acc_done = sem("acc_done")
        total_done, out_ready = sem("total_done"), sem("out_ready")

        block = ctx.enter_context(nc.Block())

        def d_view(t, row, off, n, rows, row_step, inner, inner_step):
            return bass.AP(tensor=t, offset=off, ap=[[row_step, rows], [inner_step, n], [1, inner]])

        @block.sync
        def _(sp):
            def load_xa(u, par):
                sp.dma_start(x_a[:, par, :], xa[:, bass.ds(u * N, N)]).then_inc(xa_loaded[par], 16)

            def load_xb(u, c):
                sp.dma_start(xb_z[:, c, :], xw[3 * c:3 * c + 128, bass.ds(u * N, N)]).then_inc(xb_loaded[c], 16)

            load_xa(0, 0)
            load_xb(0, 0)
            sp.dma_start(w2_d[:, 0:M * H], w2t).then_inc(w2_loaded, 16)
            sp.dma_start(pair_sb[:, :, :], w0_pairs).then_inc(w0_loaded, 16)
            load_xb(0, 1)
            load_xb(0, 2)
            sp.dma_start(w1_post[:, :], w1x).then_inc(w1_loaded, 16)
            for c in range(3, C):
                load_xb(0, c)
            load_xa(1, 1)
            for c in range(C):
                sp.wait_ge(low_done, c + 1)
                load_xb(1, c)
            sp.wait_ge(wsum_done, 1)
            sp.wait_ge(t2_cleared, 1)
            sp.wait_ge(d_stored, 16 * 4)
            for t in range(T):
                for i0, n in ((0, 32), (32, F - 32)):
                    p = F * t + i0
                    ia = i0 - t + 2
                    sp.dma_start(pair_sb[p:p + n, 0, :].rearrange("p (c j) -> p c j", j=J),
                                 d_view(d1, 0, (ia * WB + i0) * J, C, n, (WB + 1) * J, J, T * J)
                                 ).then_inc(dpair_loaded, 16)
                    c0 = 1 if t == 0 else 0
                    sp.dma_start(pair_sb[p:p + n, 1, c0 * J:].rearrange("p (c j) -> p c j", j=J),
                                 d_view(d2, 0, ((i0 + 3 * c0 + 2) * WA + ia) * J, C - c0, n, (WA + 1) * J, J,
                                        T * WA * J)).then_inc(dpair_loaded, 16)
            with sp.Fori(0, U // 2 - 1) as it:
                for par in range(2):
                    u = it * 2 + (2 + par)
                    sp.wait_ge(z_done, (it * 2 + (1 + par)) * C)
                    load_xa(u, par)
                    for c in range(C):
                        sp.wait_ge(low_done, (it * 2 + (1 + par)) * C + (c + 1))
                        load_xb(u, c)
            sp.wait_ge(out_ready, 1)
            sp.dma_start(out, out_sb[:, :]).then_inc(out_stored, 16)
            sp.wait_ge(out_stored, 16)

        @block.vector
        def _(dve):
            def form(it, m):
                u, c = divmod(m, C)
                dve.wait_ge(xb_loaded[c], it * 32 + 16 * (u + 1))
                dve.wait_ge(xa_loaded[u % 2], it * 16 + 16 * (u // 2 + 1))
                nc.vector.tensor_tensor(xb_z[0:K, c, :], x_a[0:K, u % 2, :], xb_z[0:K, c, :],
                                        ALU.mult).then_inc(z_done, 1)

            def split(it, m):
                c = m % C
                dve.wait_ge(high_done, it * BODY + (m + 1))
                dve.wait_ge(z_slots_free, it * BODY + (m + 1))
                nc.vector.tensor_tensor(z_low[0:K, m % SLOTS, :], xb_z[0:K, c, :],
                                        z_high[0:K, m % SLOTS, :].bitcast(fp32), ALU.subtract).then_inc(low_done, 1)

            def product(it, u):
                dve.wait_ge(z_slots_free, it * BODY + (SLOTS + C * (u + 1)))
                dve.wait_ge(c1_copied, it * 2 + (u + 1))
                dve.wait_ge(acc_done, it * 2 + (u + 1))
                nc.vector.tensor_tensor(prod, q_ps[u % 2][0:J, :], c1_sb[u % 2], ALU.mult).then_inc(q_psum_free, 1)
                dve.wait_ge(q_psum_free, it * 2 + (u + 3))
                nc.vector.tensor_tensor(acc[:, :], acc[:, :], prod, ALU.add).then_inc(acc_done, 1)

            def steps(it, m0):
                for m in range(m0, m0 + BODY):
                    form(it, m)
                    if m > 0:
                        if m >= 20 and (m - 20) % C == 0:
                            product(it, (m - 20) // C)
                        split(it, m - 1)

            steps(0, 0)
            with dve.Fori(0, NCH // BODY - 1) as it:
                steps(it, BODY)
            split(0, NCH - 1)
            product(0, U - 2)
            product(0, U - 1)

        @block.scalar
        def _(act):
            def round_high(it, m):
                act.wait_ge(z_done, it * BODY + (m + 1))
                act.wait_ge(z_slots_free, it * BODY + (m + 1))
                nc.scalar.activation(z_high[0:K, m % SLOTS, :], xb_z[0:K, m % C, :], ACT.Copy).then_inc(high_done, 1)

            def copy_c1(it, u):
                act.wait_ge(c1_done, it * 2 + (u + 1))
                if u >= 1:
                    act.wait_ge(q_psum_free, it * 2 + (u + 1))
                nc.scalar.activation(c1_sb[u % 2], c1_ps[u % 2][0:J, :], ACT.Copy).then_inc(c1_copied, 1)
                act.wait_ge(c1_copied, it * 2 + (u + 1))
                act.sem_inc(c1_psum_free, 1)

            def copy_v():
                act.wait_ge(v_done, 1)
                act.wait_ge(small_loaded, 48)
                nc.scalar.activation(v_sb[0:H, 0:1], v_ps[:, M - 1:M], ACT.Copy)
                nc.scalar.activation(v_sb[0:H, 2:2 + M], v_ps, ACT.Copy)
                nc.scalar.activation(v_sb[0:H, F + 2:DB], v_ps[:, 0:DB - F - 2], ACT.Copy)
                nc.scalar.activation(const_sb[:, :], const_ps, ACT.Identity, bias=linb_sb[0:1, 0:1],
                                     scale=float(D)).then_inc(v_copied, 1)

            def copy_d(g):
                n = (GI if g < NG - 1 else 1) * J
                act.wait_ge(dgroup_done, g + 1)
                nc.scalar.activation(w2_d[0:DB, g * GI * J:g * GI * J + n], d_ps[g % 4][0:DB, 0:n],
                                     ACT.Copy).then_inc(dgroup_copied, 1)

            act.dma_start(v_sb[:, :], v_init).then_inc(small_loaded, 16)
            act.dma_start(head_sb[:, :], head).then_inc(small_loaded, 16)
            act.dma_start(linb_sb[:, :], lin_b).then_inc(small_loaded, 16)
            for m in range(BODY):
                if m == 4:
                    copy_v()
                if m == 7:
                    for g in range(NG):
                        copy_d(g)
                    act.wait_ge(dgroup_copied, NG)
                    act.sem_inc(c1_psum_free, 2)
                    act.sem_inc(q_psum_free, 2)
                    act.dma_start(d1[:, 0:F * J], w2_d[0:DA, :]).then_inc(d_stored, 16)
                    act.dma_start(d1[:, F * J:], w2_d[0:DA, 0:(WB - F) * J]).then_inc(d_stored, 16)
                    act.dma_start(d2[:, 2 * J:], w2_d[0:DB, :]).then_inc(d_stored, 16)
                    act.dma_start(d2[:, 0:2 * J], w2_d[0:DB, (F - 2) * J:]).then_inc(d_stored, 16)
                if m == 20 - LAG:
                    copy_c1(0, 0)
                round_high(0, m)
            with act.Fori(0, NCH // BODY - 1) as it:
                for m in range(BODY, 2 * BODY):
                    if (m - 20 + LAG) % C == 0:
                        copy_c1(it, (m - 20 + LAG) // C)
                    round_high(it, m)
            copy_c1(0, U - 1)
            act.wait_ge(total_done, 1)
            nc.scalar.activation(out_sb[:, :], out_ps, ACT.Identity, bias=const_sb[0:1, 0:1]).then_inc(out_ready, 1)

        @block.gpsimd
        def _(pool):
            nc.gpsimd.memset(ones[:, :], 1.0).then_inc(filled, 1)
            nc.gpsimd.memset(acc[:, :], 0.0).then_inc(acc_done, 1)
            nc.gpsimd.sem_inc(z_slots_free, SLOTS)

            def weights(i, high, low, ready):
                a, b = pair_sb[0:K, 0, :], pair_sb[0:K, 1, :]
                nc.gpsimd.tensor_tensor(a, a, b, ALU.add).then_inc(wsum_done, 1)
                pool.wait_ge(wsum_done, 2 * i + 1)
                nc.gpsimd.tensor_copy(high[0:K, :], a).then_inc(whigh_done, 1)
                pool.wait_ge(whigh_done, i + 1)
                nc.gpsimd.tensor_tensor(low[0:K, :], a, high[0:K, :].bitcast(fp32), ALU.subtract).then_inc(ready, 1)

            pool.wait_ge(w0_loaded, 16)
            weights(0, wc_high, wc_low, wc_ready)
            pool.wait_ge(wc_ready, 1)
            nc.gpsimd.memset(pair_sb[0:F, 1, 0:J], 0.0).then_inc(t2_cleared, 1)
            nc.gpsimd.sem_inc(wsum_done, 1)
            pool.wait_ge(dpair_loaded, 16 * 4 * T)
            weights(1, wq_high, wq_low, wq_ready)

        @block.tensor
        def _(pe):
            def chunk_products(ps, high, low, m):
                c, slot = m % C, m % SLOTS
                for k, (w, z) in enumerate(((high, z_high), (low, z_high), (high, z_low))):
                    for h in range(2):
                        last = nc.tensor.matmul(ps[0:J, h * B:(h + 1) * B], w[0:K, c * J:(c + 1) * J],
                                                z[0:K, slot, h * B:(h + 1) * B],
                                                start=(c == 0 and k == 0), stop=(c == C - 1 and k == 2))
                return last

            def c1_chunk(it, m):
                u, c = divmod(m, C)
                pe.wait_ge(high_done, it * BODY + (m + 1))
                pe.wait_ge(low_done, it * BODY + (m + 1))
                if c == 0 and u >= 1:
                    pe.wait_ge(c1_psum_free, it * 2 + (u + 1))
                last = chunk_products(c1_ps[u % 2], wc_high, wc_low, m)
                if c == C - 1:
                    last.then_inc(c1_done, 1)

            def q_chunk(it, m):
                u, c = divmod(m, C)
                if c == 0:
                    pe.wait_ge(q_psum_free, it * 2 + (u + 1))
                chunk_products(q_ps[u % 2], wq_high, wq_low, m).then_inc(z_slots_free, 1)

            pe.wait_ge(w2_loaded, 16)
            pe.wait_ge(small_loaded, 48)
            for k in range(M):
                nc.tensor.matmul(v_ps[:, k:k + 1], w2_d[0:H, k * H:(k + 1) * H], head_sb[:, 0:1],
                                 start=True, stop=True)
            nc.tensor.matmul(const_ps, head_sb[:, 0:1], head_sb[:, 1:2], start=True, stop=True).then_inc(v_done, 1)
            pe.wait_ge(wc_ready, 1)
            for m in range(LAG):
                c1_chunk(0, m)
                if m == 3:
                    pe.wait_ge(w1_loaded, 16)
                    pe.wait_ge(v_copied, 1)
                    for g in range(NG):
                        n = (GI if g < NG - 1 else 1) * J
                        if g >= 4:
                            pe.wait_ge(dgroup_copied, g - 3)
                        nc.tensor.matmul(d_ps[g % 4][0:DB, 0:n], v_sb[:, :], w1_post[0:J, g * GI * J:g * GI * J + n],
                                         start=True, stop=True).then_inc(dgroup_done, 1)
            pe.wait_ge(wq_ready, 1)
            whole = (NCH - LAG) // BODY
            with pe.Fori(0, whole) as it:
                for m in range(LAG, LAG + BODY):
                    c1_chunk(it, m)
                    q_chunk(it, m - LAG)
            for m in range(LAG + whole * BODY, NCH):
                c1_chunk(0, m)
                q_chunk(0, m - LAG)
            for m in range(NCH - LAG, NCH):
                q_chunk(0, m)
            pe.wait_ge(filled, 1)
            pe.wait_ge(acc_done, U + 1)
            pe.wait_ge(c1_psum_free, U + 2)
            for h in range(2):
                last = nc.tensor.matmul(out_ps, ones[:, :], acc[:, h * B:(h + 1) * B], start=(h == 0), stop=(h == 1))
            last.then_inc(total_done, 1)


def kernel(r_inputs, L0_rec_W0, L0_rec_W1, L0_rec_W2, L0_rec_b0, L0_rec_b1, L0_rec_b2, L0_rec_lin_w, L0_rec_lin_b):
    import numpy as np
    import concourse.bacc as bacc
    from concourse.bass_utils import run_bass_kernel_spmd

    x, w0, w1, w2, b0, b1, b2, lw, lb = (np.asarray(a) for a in (
        r_inputs, L0_rec_W0, L0_rec_W1, L0_rec_W2, L0_rec_b0, L0_rec_b1, L0_rec_b2, L0_rec_lin_w, L0_rec_lin_b))
    f = x.dtype
    xt = np.ones((F, D * B), f)
    xt[:M] = x.transpose(1, 2, 0).reshape(M, D * B)
    p = np.arange(128)
    xa = np.ascontiguousarray(xt[(p % F - p // F) % F])
    xw = np.ascontiguousarray(xt[np.arange(128 + T * (C - 1)) % F])
    full = np.zeros((F, F, J), f)
    full[:M, :M, :H] = w0
    full[M, M, :H] = b0
    full[M, M, H] = 1
    rows = np.arange(K)
    a = (rows % F - rows // F) % F
    w0_pairs = np.zeros((128, 2, C, J), f)
    for c in range(C):
        b = (rows + T * c) % F
        w0_pairs[:K, 0, c] = full[a, b]
        w0_pairs[:K, 1, c] = full[b, a]
    w0_pairs[:F, 1, 0] = 0
    w1x = np.zeros((112, F, J), f)
    w1x[:H, :M, :H] = w1.transpose(2, 0, 1)
    w1x[:H, M, H] = b1
    w1x[H, M, :H] = lw[:H, 0]
    w2t = np.zeros((112, M, H), f)
    w2t[:H] = w2.transpose(2, 0, 1)
    v_init = np.zeros((J, DB), f)
    v_init[:H, [1, F + 1]] = lw[H:2 * H]
    v_init[H, [1, F + 1]] = 1
    arrays = {
        "xa": xa, "xw": xw, "w0_pairs": w0_pairs.reshape(128, 2, C * J), "w1x": w1x.reshape(112, F * J),
        "w2t": w2t.reshape(112, M * H), "v_init": v_init,
        "head": np.ascontiguousarray(np.stack([lw[2 * H:, 0], b2], 1)), "lin_b": lb.reshape(1, 1),
    }
    nc = bacc.Bacc("TRN2", target_bir_lowering=False, num_devices=1)
    args = [nc.dram_tensor(n, v.shape, mybir.dt.from_np(v.dtype), kind="ExternalInput").ap() for n, v in arrays.items()]
    out = nc.dram_tensor("out", (1, B), mybir.dt.float32, kind="ExternalOutput").ap()
    build(nc, *args, out)
    r = run_bass_kernel_spmd(nc, [arrays], core_ids=[0])
    return r.results[0]["out"].reshape(B, 1)
```

```python
from contextlib import ExitStack

import concourse.bass as bass
from concourse import mybir

B, M, D = 512, 40, 16
H = 100
F = M + 1
J = H + 1
T = 3
C = (F // 2 + 1) // T
K = T * F
U = D // 2
N = 2 * B
NCH = U * C
SLOTS = 2 * C
GATHER_AT = 1
LAG = 7
BODY = 2 * C
GI = 5
NG = M // GI + 1
DR = 64
DW = F + 2 + 3 * (C - 1)
SEL = (1, 2, 5, 6)
W1_CUTS = (0, 2, 4, 6, NG)
SMALL = DR + H + 3 + 128 + T * max(SEL)
WARM, WARM_2 = 20, 4
WQ_AT = (8, 9)
GATHER = [(side, t, i0, n) for i0, n in ((0, 32), (32, F - 32)) for t in range(T) for side in range(2)]
POOL_GATHERS = 3
VP = 4
VK = M // VP
WC_CUTS = (0, 1, 3, C)
WQ_CUTS = (0, 2, C)


def build(nc, xa, xw, w0_pairs, w1x, w2h, small, out):
    fp32, f32r = mybir.dt.float32, mybir.dt.float32r
    ALU, ACT = mybir.AluOpType, mybir.ActivationFunctionType

    with ExitStack() as ctx:
        def sb(name, shape, dt=fp32):
            return ctx.enter_context(nc.sbuf_tensor(name, shape, dt))

        def sem(name):
            return ctx.enter_context(nc.semaphore(name))

        z_high = sb("z_high", [128, SLOTS, N], f32r)
        z_low = sb("z_low", [128, SLOTS, N], f32r)
        xb_z = sb("xb_z", [128, C, N])
        x_a = sb("x_a", [128, 2, N])
        wc_high = sb("wc_high", [128, C * J], f32r)
        wc_low = sb("wc_low", [128, C * J], f32r)
        wq_high = sb("wq_high", [128, C * J], f32r)
        wq_low = sb("wq_low", [128, C * J], f32r)
        pair_sb = sb("pair_sb", [128, 2, C * J])
        w2_d = sb("w2_d", [112, F * J])
        w1_post = sb("w1_post", [112, F * J])
        v_kh = sb("v_kh", [H, M])
        small_sb = sb("small_sb", [112, SMALL])
        const_sb = sb("const_sb", [1, 1])
        ones = sb("ones", [J, 1])
        warm_sb = sb("warm_sb", [128, B], mybir.dt.bfloat16)
        acc = sb("acc", [J, N])
        out_sb = sb("out_sb", [1, B])
        v_sb = small_sb[0:J, 0:DR]
        lw3_rows = small_sb[0:H, DR:DR + H]
        lw3, b2 = (small_sb[0:H, DR + H + i:DR + H + i + 1] for i in range(2))
        linb = small_sb[0:1, DR + H + 2:DR + H + 3]
        select_sb = small_sb[0:F, DR + H + 3:]
        c1_sb = [w1_post[0:J, i * N:(i + 1) * N] for i in range(2)]
        prod = w1_post[0:J, 2 * N:3 * N]

        c1_ps = [ctx.enter_context(nc.psum_tensor(f"c1_ps{i}", [128, N], fp32)) for i in range(2)]
        q_ps = [ctx.enter_context(nc.psum_tensor(f"q_ps{i}", [128, N], fp32)) for i in range(2)]
        sel_ps = dict(zip(SEL, (c1_ps[1], c1_ps[0], q_ps[0], q_ps[1])))
        const_ps = q_ps[0][0:1, 0:1]
        warm_ps = q_ps[1][:, 0:B]
        d_ps = [t[:, h * B:(h + 1) * B] for t in (q_ps[1], q_ps[0]) for h in range(2)]
        out_ps = c1_ps[0][0:1, 0:B]

        d_dram = nc.dram_tensor("d_dram", [DR, DW * J], fp32, kind="Internal")

        xb_loaded = [sem(f"xb_loaded{c}") for c in range(C)]
        xa_loaded = [sem(f"xa_loaded{i}") for i in range(2)]
        w0_loaded = sem("w0_loaded")
        w1_loaded = [sem(f"w1_loaded{i}") for i in range(len(W1_CUTS) - 1)]
        w2_loaded = [sem(f"w2_loaded{i}") for i in range(VP)]
        small_loaded, selected = sem("small_loaded"), sem("selected")
        d_stored = sem("d_stored")
        dpair_loaded = [sem("dpair_loaded_sp"), sem("dpair_loaded_pool")]
        out_stored = sem("out_stored")
        w2_scaled, w2_scaled_pool = sem("w2_scaled"), sem("w2_scaled_pool")
        v_summed, v_copied = sem("v_summed"), sem("v_copied")
        const_done = sem("const_done")
        const_copied = sem("const_copied")
        dgroup_done, dgroup_copied = sem("dgroup_done"), sem("dgroup_copied")
        wc_sums, wc_highs, wc_ready = sem("wc_sums"), sem("wc_highs"), sem("wc_ready")
        wq_sums, wq_highs, wq_ready = sem("wq_sums"), sem("wq_highs"), sem("wq_ready")
        filled, equals_cleared = sem("filled"), sem("equals_cleared")
        z_done, high_done, low_done = sem("z_done"), sem("high_done"), sem("low_done")
        c1_done, c1_psum_free, c1_copied = sem("c1_done"), sem("c1_psum_free"), sem("c1_copied")
        z_slots_free, q_psum_free = sem("z_slots_free"), sem("q_psum_free")
        acc_done = sem("acc_done")
        last_q_done = sem("last_q_done")
        last_done, total_done, out_ready = sem("last_done"), sem("total_done"), sem("out_ready")

        block = ctx.enter_context(nc.Block())

        def w2_piece(i):
            return w2_d[0:H, i * VK * H:(i + 1) * VK * H].rearrange("h (k g) -> h k g", g=H)

        lw3_piece = lw3_rows.unsqueeze(1).to_broadcast([H, VK, H])

        def d_rows(row, column, n, chunks, row_step, chunk_step):
            return bass.AP(tensor=d_dram, offset=(row * DW + column) * J,
                           ap=[[row_step * J, n], [chunk_step * J, chunks], [1, J]])

        def gather_d(eng, pieces, loaded):
            eng.wait_ge(equals_cleared, 1)
            eng.wait_ge(d_stored, 16 * 4)
            for side, t, i0, n in pieces:
                p, a, b = F * t + i0, i0 - t + 2, i0 + 2
                c0 = 1 if side == 1 and t == 0 else 0
                src = d_rows(a, b, n, C, DW + 1, T) if side == 0 else d_rows(b + T * c0, a, n, C - c0, DW + 1, T * DW)
                eng.dma_start(pair_sb[p:p + n, side, c0 * J:].rearrange("p (c j) -> p c j", j=J), src
                              ).then_inc(loaded, 16)

        @block.sync
        def _(sp):
            def load_xa(u, par):
                sp.dma_start(x_a[:, par, :], xa[:, bass.ds(u * N, N)]).then_inc(xa_loaded[par], 16)

            def load_xb(u, c):
                sp.dma_start(xb_z[:, c, :], xw[T * c:T * c + 128, bass.ds(u * N, N)]).then_inc(xb_loaded[c], 16)

            def load_w0():
                sp.dma_start(pair_sb[:, :, :], w0_pairs).then_inc(w0_loaded, 16)

            def load_w2(i):
                cols = slice(i * VK * H, (i + 1) * VK * H)
                sp.dma_start(w2_d[:, cols], w2h[:, cols]).then_inc(w2_loaded[i], 16)

            def load_w1(i):
                cols = slice(W1_CUTS[i] * GI * J, min(W1_CUTS[i + 1] * GI, F) * J)
                sp.dma_start(w1_post[:, cols], w1x[:, cols]).then_inc(w1_loaded[i], 16)

            sp.dma_start(small_sb[:, :], small).then_inc(small_loaded, 16)
            for i in range(VP):
                load_w2(i)
            load_xa(0, 0)
            load_xb(0, 0)
            for i in range(len(W1_CUTS) - 1):
                load_w1(i)
            load_w0()
            def store_d(column, i, n, rows=DR):
                sp.dma_start(d_dram[0:rows, column * J:(column + n) * J], w2_d[0:rows, i * J:(i + n) * J]
                             ).then_inc(d_stored, 16)

            load_xb(0, 3)
            load_xb(0, 4)
            sp.wait_ge(dgroup_copied, 4)
            store_d(2, 0, 4 * GI)
            store_d(F + 2, 0, T * (C - 1), 48)
            sp.wait_ge(dgroup_copied, NG)
            store_d(2 + 4 * GI, 4 * GI, F - 4 * GI)
            store_d(0, F - 2, 2)
            load_xa(1, 1)
            for c in range(C):
                if c == GATHER_AT:
                    gather_d(sp, GATHER[:-POOL_GATHERS], dpair_loaded[0])
                sp.wait_ge(low_done, c + 1)
                load_xb(1, c)
            with sp.Fori(0, U // 2 - 1) as it:
                for par in range(2):
                    u = it * 2 + (2 + par)
                    sp.wait_ge(z_done, (it * 2 + (1 + par)) * C)
                    load_xa(u, par)
                    for c in range(C):
                        sp.wait_ge(low_done, (it * 2 + (1 + par)) * C + (c + 1))
                        load_xb(u, c)
            sp.wait_ge(out_ready, 1)
            sp.dma_start(out, out_sb[:, :]).then_inc(out_stored, 16)
            sp.wait_ge(out_stored, 16)

        @block.vector
        def _(dve):
            def scale_w2(i):
                dve.wait_ge(w2_loaded[i], 16)
                nc.vector.tensor_tensor(w2_piece(i), w2_piece(i), lw3_piece, ALU.mult).then_inc(w2_scaled, 1)

            def sum_v(i, scaled, n):
                dve.wait_ge(scaled, n)
                nc.vector.tensor_reduce(out=v_kh[:, i * VK:(i + 1) * VK], in_=w2_piece(i), op=ALU.add,
                                        axis=mybir.AxisListType.X).then_inc(v_summed, 1)

            def form(it, m):
                u, c = divmod(m, C)
                dve.wait_ge(xa_loaded[u % 2], it * 16 + 16 * (u // 2 + 1))
                if m in SEL:
                    dve.wait_ge(selected, SEL.index(m) + 1)
                    x_b = sel_ps[m][0:K, :]
                else:
                    dve.wait_ge(xb_loaded[c], it * 32 + 16 * (u + (0 if c in SEL else 1)))
                    x_b = xb_z[0:K, c, :]
                nc.vector.tensor_tensor(xb_z[0:K, c, :], x_a[0:K, u % 2, :], x_b, ALU.mult).then_inc(z_done, 1)

            def split(it, m):
                c = m % C
                dve.wait_ge(high_done, it * BODY + (m + 1))
                dve.wait_ge(z_slots_free, it * BODY + (m + 1))
                nc.vector.tensor_tensor(z_low[0:K, m % SLOTS, :], xb_z[0:K, c, :],
                                        z_high[0:K, m % SLOTS, :].bitcast(fp32), ALU.subtract).then_inc(low_done, 1)

            def product(it, u):
                dve.wait_ge(z_slots_free, it * BODY + (SLOTS + C * (u + 1)))
                dve.wait_ge(c1_copied, it * 2 + (u + 1))
                dve.wait_ge(acc_done, it * 2 + (u + 1))
                nc.vector.tensor_tensor(prod, q_ps[u % 2][0:J, :], c1_sb[u % 2], ALU.mult).then_inc(q_psum_free, 1)
                dve.wait_ge(q_psum_free, it * 2 + (u + 3))
                nc.vector.tensor_tensor(acc[:, :], acc[:, :], prod, ALU.add).then_inc(acc_done, 1)

            def last_product(h):
                cols = slice(h * B, (h + 1) * B)
                nc.vector.tensor_tensor(prod[:, cols], q_ps[1][0:J, cols], c1_sb[1][:, cols],
                                        ALU.mult).then_inc(last_done, 1)

            def steps(it, m0):
                for m in range(m0, m0 + BODY):
                    form(it, m)
                    if m > 0:
                        if m >= 20 and (m - 20) % C == 0:
                            product(it, (m - 20) // C)
                        split(it, m - 1)

            dve.wait_ge(small_loaded, 16)
            scale_w2(0)
            sum_v(0, w2_scaled, 1)
            scale_w2(1)
            sum_v(1, w2_scaled, 2)
            scale_w2(3)
            sum_v(2, w2_scaled_pool, 1)
            sum_v(3, w2_scaled, 3)
            steps(0, 0)
            with dve.Fori(0, NCH // BODY - 1) as it:
                steps(it, BODY)
            split(0, NCH - 1)
            product(0, U - 2)
            dve.wait_ge(acc_done, U)
            nc.vector.tensor_tensor(acc[:, 0:B], acc[:, 0:B], acc[:, B:N], ALU.add).then_inc(acc_done, 1)
            dve.wait_ge(c1_copied, U)
            dve.wait_ge(acc_done, U)
            for h in range(2):
                dve.wait_ge(last_q_done, h + 1)
                last_product(h)

        @block.scalar
        def _(act):
            def round_high(it, m):
                act.wait_ge(z_done, it * BODY + (m + 1))
                act.wait_ge(z_slots_free, it * BODY + (m + 1))
                nc.scalar.activation(z_high[0:K, m % SLOTS, :], xb_z[0:K, m % C, :], ACT.Copy).then_inc(high_done, 1)

            def copy_c1(it, u):
                act.wait_ge(c1_done, it * 2 + (u + 1))
                if u >= 1:
                    act.wait_ge(q_psum_free, it * 2 + (u + 1))
                nc.scalar.activation(c1_sb[u % 2], c1_ps[u % 2][0:J, :], ACT.Copy).then_inc(c1_copied, 1)
                act.wait_ge(c1_copied, it * 2 + (u + 1))
                act.sem_inc(c1_psum_free, 1)

            def copy_v():
                act.wait_ge(v_summed, VP)
                nc.scalar.activation(v_sb[0:H, 0:1], v_kh[:, M - 1:M], ACT.Copy)
                nc.scalar.activation(v_sb[0:H, 2:2 + M], v_kh[:, :], ACT.Copy)
                nc.scalar.activation(v_sb[0:H, F + 2:DR], v_kh[:, 0:DR - F - 2], ACT.Copy).then_inc(v_copied, 1)

            def copy_d(g):
                n = (GI if g < NG - 1 else 1) * J
                act.wait_ge(dgroup_done, g + 1)
                nc.scalar.activation(w2_d[0:DR, g * GI * J:g * GI * J + n], d_ps[g % 4][0:DR, 0:n],
                                     ACT.Copy).then_inc(dgroup_copied, 1)

            def weights_high(i, cuts, sums, high, highs):
                cols = slice(cuts[i] * J, cuts[i + 1] * J)
                act.wait_ge(sums, i + 1)
                nc.scalar.activation(high[0:K, cols], pair_sb[0:K, 0, cols], ACT.Copy).then_inc(highs, 1)

            act.wait_ge(const_done, 1)
            nc.scalar.activation(const_sb[:, :], const_ps, ACT.Identity, bias=linb,
                                 scale=float(D)).then_inc(const_copied, 1)

            copy_v()
            round_high(0, 0)
            copy_d(0)
            round_high(0, 1)
            for g in range(1, 5):
                copy_d(g)
            weights_high(0, WC_CUTS, wc_sums, wc_high, wc_highs)
            copy_d(5)
            copy_d(6)
            round_high(0, 2)
            copy_d(7)
            copy_d(8)
            weights_high(1, WC_CUTS, wc_sums, wc_high, wc_highs)
            round_high(0, 3)
            weights_high(2, WC_CUTS, wc_sums, wc_high, wc_highs)
            act.wait_ge(dgroup_copied, NG)
            for m in range(4, BODY):
                if m == 7:
                    act.wait_ge(z_done, C)
                    act.sem_inc(c1_psum_free, 2)
                    act.sem_inc(q_psum_free, 2)
                if m == 20 - LAG:
                    copy_c1(0, 0)
                for i in range(len(WQ_CUTS) - 1):
                    if WQ_AT[i] == m:
                        weights_high(i, WQ_CUTS, wq_sums, wq_high, wq_highs)
                round_high(0, m)
            with act.Fori(0, NCH // BODY - 1) as it:
                for m in range(BODY, 2 * BODY):
                    if (m - 20 + LAG) % C == 0:
                        copy_c1(it, (m - 20 + LAG) // C)
                    round_high(it, m)
            copy_c1(0, U - 1)
            act.wait_ge(total_done, 1)
            nc.scalar.activation(out_sb[:, :], out_ps, ACT.Identity, bias=const_sb[0:1, 0:1]).then_inc(out_ready, 1)

        @block.gpsimd
        def _(pool):
            nc.gpsimd.memset(ones[:, :], 1.0)
            nc.gpsimd.memset(warm_sb[:, :], 0.0).then_inc(filled, 1)
            nc.gpsimd.memset(acc[:, :], 0.0).then_inc(acc_done, 1)
            nc.gpsimd.sem_inc(z_slots_free, SLOTS)

            def weights(cuts, high, low, sums, highs, ready):
                for i in range(len(cuts) - 1):
                    cols = slice(cuts[i] * J, cuts[i + 1] * J)
                    nc.gpsimd.tensor_tensor(pair_sb[0:K, 0, cols], pair_sb[0:K, 0, cols], pair_sb[0:K, 1, cols],
                                            ALU.add).then_inc(sums, 1)
                    low_half(i, cuts, high, low, highs, ready)

            def low_half(i, cuts, high, low, highs, ready):
                cols = slice(cuts[i] * J, cuts[i + 1] * J)
                pool.wait_ge(highs, i + 1)
                nc.gpsimd.tensor_tensor(low[0:K, cols], pair_sb[0:K, 0, cols], high[0:K, cols].bitcast(fp32),
                                        ALU.subtract).then_inc(ready, 1)

            pool.wait_ge(small_loaded, 16)
            pool.wait_ge(w2_loaded[2], 16)
            nc.gpsimd.tensor_tensor(w2_piece(2), w2_piece(2), lw3_piece, ALU.mult).then_inc(w2_scaled_pool, 1)
            pool.wait_ge(w0_loaded, 16)
            weights(WC_CUTS, wc_high, wc_low, wc_sums, wc_highs, wc_ready)
            pool.wait_ge(wc_ready, len(WC_CUTS) - 1)
            nc.gpsimd.memset(pair_sb[0:F, 1, 0:J], 0.0).then_inc(equals_cleared, 1)
            gather_d(pool, GATHER[-POOL_GATHERS:], dpair_loaded[1])
            pool.wait_ge(dpair_loaded[0], 16 * (len(GATHER) - POOL_GATHERS))
            pool.wait_ge(dpair_loaded[1], 16 * POOL_GATHERS)
            weights(WQ_CUTS, wq_high, wq_low, wq_sums, wq_highs, wq_ready)

        @block.tensor
        def _(pe):
            def chunk_products(ps, high, low, m):
                c, slot = m % C, m % SLOTS
                for k, (w, z) in enumerate(((high, z_high), (low, z_high), (high, z_low))):
                    for h in range(2):
                        last = nc.tensor.matmul(ps[0:J, h * B:(h + 1) * B], w[0:K, c * J:(c + 1) * J],
                                                z[0:K, slot, h * B:(h + 1) * B],
                                                start=(c == 0 and k == 0), stop=(c == C - 1 and k == 2))
                return last

            def half(ps, high, low, m, h):
                c, slot, cols = m % C, m % SLOTS, slice(h * B, (h + 1) * B)
                for k, (w, z) in enumerate(((high, z_high), (low, z_high), (high, z_low))):
                    last = nc.tensor.matmul(ps[0:J, cols], w[0:K, c * J:(c + 1) * J], z[0:K, slot, cols],
                                            start=False, stop=(k == 2))
                return last

            def c1_chunk(it, m):
                u, c = divmod(m, C)
                if m == 0:
                    pe.wait_ge(z_done, SEL[1] + 1)
                if m in WC_CUTS[:-1]:
                    pe.wait_ge(wc_ready, WC_CUTS.index(m) + 1)
                pe.wait_ge(high_done, it * BODY + (m + 1))
                pe.wait_ge(low_done, it * BODY + (m + 1))
                if c == 0 and u >= 1:
                    pe.wait_ge(c1_psum_free, it * 2 + (u + 1))
                last = chunk_products(c1_ps[u % 2], wc_high, wc_low, m)
                if c == C - 1:
                    last.then_inc(c1_done, 1)

            def q_chunk(it, m):
                u, c = divmod(m, C)
                if m in WQ_CUTS[:-1]:
                    pe.wait_ge(wq_ready, WQ_CUTS.index(m) + 1)
                if c == 0:
                    pe.wait_ge(q_psum_free, it * 2 + (u + 1))
                chunk_products(q_ps[u % 2], wq_high, wq_low, m).then_inc(z_slots_free, 1)

            def select_xb(c):
                pe.wait_ge(xa_loaded[0], 16)
                pe.wait_ge(small_loaded, 16)
                for h in range(2):
                    last = nc.tensor.matmul(sel_ps[c][:, h * B:(h + 1) * B], select_sb[:, T * c:T * c + 128],
                                            x_a[0:F, 0, h * B:(h + 1) * B], start=True, stop=True)
                last.then_inc(selected, 1)

            def constant():
                nc.tensor.matmul(const_ps, lw3, b2, start=True, stop=True
                                 ).then_inc(const_done, 1)

            def d_group(g):
                n = (GI if g < NG - 1 else 1) * J
                if g == 0:
                    pe.wait_ge(v_copied, 1)
                    pe.wait_ge(const_copied, 1)
                if g in W1_CUTS:
                    pe.wait_ge(w1_loaded[W1_CUTS.index(g)], 16)
                if g >= 4:
                    pe.wait_ge(dgroup_copied, g - 3)
                nc.tensor.matmul(d_ps[g % 4][0:DR, 0:n], v_sb[:, :], w1_post[0:J, g * GI * J:g * GI * J + n],
                                 start=True, stop=True).then_inc(dgroup_done, 1)

            pe.wait_ge(small_loaded, 16)
            constant()
            pe.wait_ge(filled, 1)
            for _ in range(WARM):
                nc.tensor.matmul(warm_ps, warm_sb[:, 0:128], warm_sb[:, :], start=True, stop=True)
            select_xb(SEL[0])
            select_xb(SEL[1])
            for _ in range(WARM_2):
                nc.tensor.matmul(warm_ps, warm_sb[:, 0:128], warm_sb[:, :], start=True, stop=True)
            for g in range(NG):
                d_group(g)
            pe.wait_ge(dgroup_copied, NG)
            select_xb(SEL[2])
            select_xb(SEL[3])
            for m in range(LAG):
                c1_chunk(0, m)
            whole = (NCH - LAG) // BODY
            with pe.Fori(0, whole) as it:
                for m in range(LAG, LAG + BODY):
                    c1_chunk(it, m)
                    q_chunk(it, m - LAG)
            for m in range(LAG + whole * BODY, NCH):
                c1_chunk(0, m)
                q_chunk(0, m - LAG)
            for m in range(NCH - LAG, NCH - 1):
                q_chunk(0, m)
            pe.wait_ge(acc_done, U + 1)
            pe.wait_ge(c1_psum_free, U + 2)
            nc.tensor.matmul(out_ps, ones[:, :], acc[:, 0:B], start=True, stop=False)
            for h in range(2):
                half(q_ps[1], wq_high, wq_low, NCH - 1, h).then_inc(last_q_done, 1)
            for h in range(2):
                pe.wait_ge(last_done, h + 1)
                last = nc.tensor.matmul(out_ps, ones[:, :], prod[:, h * B:(h + 1) * B], start=False, stop=(h == 1))
            last.then_inc(total_done, 1)


def kernel(r_inputs, L0_rec_W0, L0_rec_W1, L0_rec_W2, L0_rec_b0, L0_rec_b1, L0_rec_b2, L0_rec_lin_w, L0_rec_lin_b):
    import numpy as np
    import concourse.bacc as bacc
    from concourse.bass_utils import run_bass_kernel_spmd

    x, w0, w1, w2, b0, b1, b2, lw, lb = (np.asarray(a) for a in (
        r_inputs, L0_rec_W0, L0_rec_W1, L0_rec_W2, L0_rec_b0, L0_rec_b1, L0_rec_b2, L0_rec_lin_w, L0_rec_lin_b))
    f = x.dtype
    xt = np.ones((F, D * B), f)
    xt[:M] = x.transpose(1, 2, 0).reshape(M, D * B)
    p = np.arange(128)
    xa = np.ascontiguousarray(xt[(p % F - p // F) % F])
    xw = np.ascontiguousarray(xt[np.arange(128 + T * (C - 1)) % F])
    full = np.zeros((F, F, J), f)
    full[:M, :M, :H] = w0
    full[M, M, :H] = b0
    full[M, M, H] = 1
    rows = np.arange(K)
    a = (rows % F - rows // F) % F
    w0_pairs = np.zeros((128, 2, C, J), f)
    for c in range(C):
        b = (rows + T * c) % F
        w0_pairs[:K, 0, c] = full[a, b]
        w0_pairs[:K, 1, c] = full[b, a]
    w0_pairs[:F, 1, 0] = 0
    w1x = np.zeros((112, F, J), f)
    w1x[:H, :M, :H] = w1.transpose(2, 0, 1)
    w1x[:H, M, H] = b1
    w1x[H, M, :H] = lw[:H, 0]
    w2h = np.zeros((112, M, H), f)
    w2h[:H] = w2.transpose(1, 0, 2)
    small = np.zeros((112, SMALL), f)
    small[:H, [1, F + 1]] = lw[H:2 * H]
    small[H, [1, F + 1]] = 1
    small[:H, DR:DR + H] = lw[2 * H:, 0]
    small[:H, DR + H] = lw[2 * H:, 0]
    small[:H, DR + H + 1] = b2
    small[0, DR + H + 2] = lb[0]
    small[:F, DR + H + 3:] = np.arange(F)[:, None] == np.arange(128 + T * max(SEL))[None] % F
    arrays = {
        "xa": xa, "xw": xw, "w0_pairs": w0_pairs.reshape(128, 2, C * J), "w1x": w1x.reshape(112, F * J),
        "w2h": w2h.reshape(112, M * H), "small": small,
    }
    nc = bacc.Bacc("TRN2", target_bir_lowering=False, num_devices=1)
    args = {n: nc.dram_tensor(n, v.shape, mybir.dt.from_np(v.dtype), kind="ExternalInput").ap()
            for n, v in arrays.items()}
    out = nc.dram_tensor("out", (1, B), mybir.dt.float32, kind="ExternalOutput").ap()
    build(nc, out=out, **args)
    r = run_bass_kernel_spmd(nc, [arrays], core_ids=[0])
    return r.results[0]["out"].reshape(B, 1)
```

```python
from contextlib import ExitStack

import concourse.bass as bass
from concourse import mybir

B, M, D = 512, 40, 16
H = 100
F = M + 1
J = H + 1
T = 3
C = (F // 2 + 1) // T
K = T * F
U = D // 2
N = 2 * B
NCH = U * C
SLOTS = 2 * C
LAG = 7
BODY = 2 * C
PRODUCT_AT = 20
LATE = C + 2

VP = 4
VK = M // VP
V_PE, V_DVE = (0, 3), (1, 2)
GI = 5
NG = M // GI + 1
W1_CUTS = (0, 2, 4, 6, NG)
DR = 64
DW = F + 2 + T * (C - 1)
DS = 4
WC_CUTS = (0, 1, 3, C)
WQ_CUTS = (0, 2, C)
WQ_AT = (8, 9)
GATHER = [(side, t, piece) for piece in range(len(WQ_CUTS) - 1) for t in range(T) for side in range(2)]
POOL_GATHERS = [GATHER[i] for i in (4, 5, 11)]
SP_GATHERS = [g for g in GATHER if g not in POOL_GATHERS]

LOW_AT = 64
XS = LOW_AT + F + 1
SW = 128 + T * (C - 1)
WARM = 6
SMALL = DR + H + 3 + SW


def build(nc, xa, xw, w0_pairs, w1x, w2h, small, out):
    fp32, f32r = mybir.dt.float32, mybir.dt.float32r
    ALU, ACT = mybir.AluOpType, mybir.ActivationFunctionType

    with ExitStack() as ctx:
        def sb(name, shape, dt=fp32):
            return ctx.enter_context(nc.sbuf_tensor(name, shape, dt))

        def sem(name):
            return ctx.enter_context(nc.semaphore(name))

        z_high = sb("z_high", [128, SLOTS, N], f32r)
        z_low = sb("z_low", [128, SLOTS, N], f32r)
        xb_z = sb("xb_z", [128, C, N])
        x_a = sb("x_a", [128, 2, N])
        wc_high = sb("wc_high", [128, C * J], f32r)
        wc_low = sb("wc_low", [128, C * J], f32r)
        wq_high = sb("wq_high", [128, C * J], f32r)
        wq_low = sb("wq_low", [128, C * J], f32r)
        pair_sb = sb("pair_sb", [128, 2, C * J])
        w2_d = sb("w2_d", [112, F * J])
        w1_post = sb("w1_post", [112, F * J])
        small_sb = sb("small_sb", [112, SMALL])
        select_r = sb("select_r", [XS, SW], f32r)
        const_sb = sb("const_sb", [1, 1])
        ones = sb("ones", [J, 1])
        warm_sb = sb("warm_sb", [128, B], mybir.dt.bfloat16)
        acc = sb("acc", [J, N])
        out_sb = sb("out_sb", [1, B])
        v_sb = small_sb[0:J, 0:DR]
        lw3_rows = small_sb[0:H, DR:DR + H]
        lw3, b2 = (small_sb[0:H, DR + H + i:DR + H + i + 1] for i in range(2))
        linb = small_sb[0:1, DR + H + 2:DR + H + 3]
        select_sb = small_sb[0:XS, DR + H + 3:]
        x_split = z_high[:, SLOTS - 1, :]
        c1_sb = [w1_post[0:J, i * N:(i + 1) * N] for i in range(2)]
        prod = w1_post[0:J, 2 * N:3 * N]

        c1_ps = [ctx.enter_context(nc.psum_tensor(f"c1_ps{i}", [128, N], fp32)) for i in range(2)]
        q_ps = [ctx.enter_context(nc.psum_tensor(f"q_ps{i}", [128, N], fp32)) for i in range(2)]
        sel_ps = (None, c1_ps[1], c1_ps[0], c1_ps[1], c1_ps[1], q_ps[0], q_ps[1])
        const_ps = q_ps[0][0:1, 0:1]
        v_ps = dict(zip(V_PE, (q_ps[0][0:H, B:B + VK], c1_ps[0][0:H, 0:VK])))
        warm_ps = q_ps[1][:, 0:B]
        d_ps = [t[:, h * B:(h + 1) * B] for t in (q_ps[1], q_ps[0]) for h in range(2)]
        out_ps = c1_ps[0][0:1, 0:B]

        d_dram = nc.dram_tensor("d_dram", [DR, DW * J], fp32, kind="Internal")

        xb_loaded = [sem(f"xb_loaded{c}") for c in range(C)]
        xa_loaded = [sem(f"xa_loaded{i}") for i in range(2)]
        w0_loaded = sem("w0_loaded")
        w1_loaded = [sem(f"w1_loaded{i}") for i in range(len(W1_CUTS) - 1)]
        w2_loaded = [sem(f"w2_loaded{i}") for i in range(VP)]
        small_loaded, selected = sem("small_loaded"), sem("selected")
        d_stored = sem("d_stored")
        dpair_loaded = [sem(f"dpair_loaded{i}") for i in range(len(WQ_CUTS) - 1)]
        dpair_loaded_pool = [sem(f"dpair_loaded_pool{i}") for i in range(len(WQ_CUTS) - 1)]
        out_stored = sem("out_stored")
        w2_scaled, v_multiplied = sem("w2_scaled"), sem("v_multiplied")
        v_summed, v_copied = sem("v_summed"), sem("v_copied")
        const_done = sem("const_done")
        const_copied = sem("const_copied")
        dgroup_done, dgroup_copied = sem("dgroup_done"), sem("dgroup_copied")
        wc_sums, wc_highs, wc_ready = sem("wc_sums"), sem("wc_highs"), sem("wc_ready")
        wq_sums, wq_highs, wq_ready = sem("wq_sums"), sem("wq_highs"), sem("wq_ready")
        filled, equals_cleared = sem("filled"), sem("equals_cleared")
        z_done, high_done, low_done = sem("z_done"), sem("high_done"), sem("low_done")
        c1_done, c1_psum_free, c1_copied = sem("c1_done"), sem("c1_psum_free"), sem("c1_copied")
        z_slots_free, q_psum_free = sem("z_slots_free"), sem("q_psum_free")
        xa_high, xa_split = sem("xa_high"), sem("xa_split")
        acc_done = sem("acc_done")
        last_q_done = sem("last_q_done")
        last_done, total_done, out_ready = sem("last_done"), sem("total_done"), sem("out_ready")

        block = ctx.enter_context(nc.Block())

        def w2_piece(i):
            return w2_d[0:H, i * VK * H:(i + 1) * VK * H].rearrange("h (k g) -> h k g", g=H)

        lw3_piece = lw3_rows.unsqueeze(1).to_broadcast([H, VK, H])

        def gather_d(eng, pieces, loaded):
            for side, t, piece in pieces:
                c0 = max(WQ_CUTS[piece], 1 if side == 1 and t == 0 else 0)
                c1 = WQ_CUTS[piece + 1]
                a, b = 2 - t, 2 + T * c0
                row, column, c_step = (a, b, T) if side == 0 else (b, a, T * DW)
                src = bass.AP(tensor=d_dram, offset=(row * DW + column) * J,
                              ap=[[(DW + 1) * J, F], [c_step * J, c1 - c0], [1, J]])
                eng.dma_start(pair_sb[F * t:F * (t + 1), side, c0 * J:c1 * J].rearrange("p (c j) -> p c j", j=J), src
                              ).then_inc(loaded[piece], 16)

        @block.sync
        def _(sp):
            def load_xa(u, par):
                sp.dma_start(x_a[:, par, :], xa[:, bass.ds(u * N, N)]).then_inc(xa_loaded[par], 16)

            def load_xb(u, c):
                sp.dma_start(xb_z[:, c, :], xw[T * c:T * c + 128, bass.ds(u * N, N)]).then_inc(xb_loaded[c], 16)

            def load_w0():
                sp.dma_start(pair_sb[:, :, :], w0_pairs).then_inc(w0_loaded, 16)

            def load_w2(i):
                cols = slice(i * VK * H, (i + 1) * VK * H)
                sp.dma_start(w2_d[:, cols], w2h[:, cols]).then_inc(w2_loaded[i], 16)

            def load_w1(i):
                cols = slice(W1_CUTS[i] * GI * J, min(W1_CUTS[i + 1] * GI, F) * J)
                sp.dma_start(w1_post[:, cols], w1x[:, cols]).then_inc(w1_loaded[i], 16)

            def store_d(column, i, n, rows=DR):
                sp.dma_start(d_dram[0:rows, column * J:(column + n) * J], w2_d[0:rows, i * J:(i + n) * J]
                             ).then_inc(d_stored, 16)

            sp.dma_start(small_sb[:, :], small).then_inc(small_loaded, 16)
            for i in range(VP):
                load_w2(i)
            load_xa(0, 0)
            load_xb(0, 0)
            for i in range(len(W1_CUTS) - 1):
                load_w1(i)
            load_w0()
            load_xa(1, 1)
            sp.wait_ge(dgroup_copied, 4)
            store_d(2, 0, 4 * GI)
            store_d(F + 2, 0, T * (C - 1), 48)
            sp.wait_ge(low_done, 1)
            load_xb(1, 0)
            sp.wait_ge(dgroup_copied, NG)
            store_d(2 + 4 * GI, 4 * GI, F - 4 * GI)
            store_d(0, F - 2, 2)
            for c in range(1, C):
                if C + c == LATE:
                    sp.wait_ge(equals_cleared, 1)
                    sp.wait_ge(d_stored, 16 * DS)
                    gather_d(sp, SP_GATHERS, dpair_loaded)
                sp.wait_ge(low_done, c + 1)
                load_xb(1, c)
            with sp.Fori(0, U // 2 - 1) as it:
                for par in range(2):
                    u = it * 2 + (2 + par)
                    sp.wait_ge(z_done, (it * 2 + (1 + par)) * C)
                    load_xa(u, par)
                    for c in range(C):
                        sp.wait_ge(low_done, (it * 2 + (1 + par)) * C + (c + 1))
                        load_xb(u, c)
            sp.wait_ge(out_ready, 1)
            sp.dma_start(out, out_sb[:, :]).then_inc(out_stored, 16)
            sp.wait_ge(out_stored, 16)

        @block.vector
        def _(dve):
            def make_v(i):
                dve.wait_ge(w2_loaded[i], 16)
                nc.vector.tensor_tensor(w2_piece(i), w2_piece(i), lw3_piece, ALU.mult).then_inc(w2_scaled, 1)
                dve.wait_ge(w2_scaled, V_DVE.index(i) + 1)
                nc.vector.tensor_reduce(out=v_sb[0:H, 2 + i * VK:2 + (i + 1) * VK], in_=w2_piece(i), op=ALU.add,
                                        axis=mybir.AxisListType.X).then_inc(v_summed, 1)

            def form(it, m):
                u, c = divmod(m, C)
                dve.wait_ge(xa_loaded[u % 2], it * 16 + 16 * (u // 2 + 1))
                if 0 < m < C:
                    dve.wait_ge(selected, m)
                    x_b = sel_ps[m][0:K, :]
                else:
                    dve.wait_ge(xb_loaded[c], it * 32 + 16 * (u if c > 0 else u + 1))
                    x_b = xb_z[0:K, c, :]
                nc.vector.tensor_tensor(xb_z[0:K, c, :], x_a[0:K, u % 2, :], x_b, ALU.mult).then_inc(z_done, 1)

            def split(it, m):
                c = m % C
                dve.wait_ge(high_done, it * BODY + (m + 1))
                dve.wait_ge(z_slots_free, it * BODY + (m + 1))
                nc.vector.tensor_tensor(z_low[0:K, m % SLOTS, :], xb_z[0:K, c, :],
                                        z_high[0:K, m % SLOTS, :].bitcast(fp32), ALU.subtract).then_inc(low_done, 1)

            def product(it, u):
                dve.wait_ge(z_slots_free, it * BODY + (SLOTS + C * (u + 1)))
                dve.wait_ge(c1_copied, it * 2 + (u + 1))
                dve.wait_ge(acc_done, it * 2 + (u + 1))
                nc.vector.tensor_tensor(prod, q_ps[u % 2][0:J, :], c1_sb[u % 2], ALU.mult).then_inc(q_psum_free, 1)
                dve.wait_ge(q_psum_free, it * 2 + (u + 3))
                nc.vector.tensor_tensor(acc[:, :], acc[:, :], prod, ALU.add).then_inc(acc_done, 1)

            def last_product(cols):
                nc.vector.tensor_tensor(prod[:, cols], q_ps[1][0:J, cols], c1_sb[1][:, cols],
                                        ALU.mult).then_inc(last_done, 1)

            def products(it, m0):
                for m in range(m0, m0 + BODY):
                    if m != LATE:
                        form(it, m)
                    if m >= PRODUCT_AT and (m - PRODUCT_AT) % C == 0:
                        product(it, (m - PRODUCT_AT) // C)
                    if m > 0:
                        split(it, m - 1)
                    if m == LATE:
                        form(it, m)

            dve.wait_ge(small_loaded, 16)
            for i in V_DVE:
                make_v(i)
            dve.wait_ge(xa_high, 1)
            nc.vector.tensor_tensor(x_split[LOW_AT:XS], x_a[LOW_AT:XS, 0, :], x_split[LOW_AT:XS].bitcast(fp32),
                                    ALU.subtract).then_inc(xa_split, 1)
            products(0, 0)
            with dve.Fori(0, NCH // BODY - 1) as it:
                products(it, BODY)
            split(0, NCH - 1)
            product(0, U - 2)
            dve.wait_ge(acc_done, U)
            nc.vector.tensor_tensor(acc[:, 0:B], acc[:, 0:B], acc[:, B:N], ALU.add).then_inc(acc_done, 1)
            dve.wait_ge(c1_copied, U)
            dve.wait_ge(last_q_done, 1)
            last_product(slice(0, B))
            dve.wait_ge(last_done, 1)
            dve.wait_ge(acc_done, U + 1)
            nc.vector.tensor_tensor(acc[:, 0:B], acc[:, 0:B], prod[:, 0:B], ALU.add).then_inc(acc_done, 1)
            dve.wait_ge(last_q_done, 2)
            last_product(slice(B, B + B // 2))
            last_product(slice(B + B // 2, N))

        @block.scalar
        def _(act):
            def round_high(it, m):
                act.wait_ge(z_done, it * BODY + (m + 1))
                act.wait_ge(z_slots_free, it * BODY + (m + 1))
                nc.scalar.activation(z_high[0:K, m % SLOTS, :], xb_z[0:K, m % C, :], ACT.Copy).then_inc(high_done, 1)

            def copy_c1(it, u):
                act.wait_ge(c1_done, it * 2 + (u + 1))
                if u >= 1:
                    act.wait_ge(q_psum_free, it * 2 + (u + 1))
                nc.scalar.activation(c1_sb[u % 2], c1_ps[u % 2][0:J, :], ACT.Copy).then_inc(c1_copied, 1)
                act.wait_ge(c1_copied, it * 2 + (u + 1))
                act.sem_inc(c1_psum_free, 1)

            def copy_v(column, k0, k1):
                i = k0 // VK
                src = v_ps[i][:, k0 - i * VK:k1 - i * VK] if i in V_PE else v_sb[0:H, 2 + k0:2 + k1]
                return nc.scalar.activation(v_sb[0:H, column:column + k1 - k0], src, ACT.Copy)

            def copy_d(g):
                n = (GI if g < NG - 1 else 1) * J
                act.wait_ge(dgroup_done, g + 1)
                nc.scalar.activation(w2_d[0:DR, g * GI * J:g * GI * J + n], d_ps[g % 4][0:DR, 0:n],
                                     ACT.Copy).then_inc(dgroup_copied, 1)

            def weights_high(i, cuts, sums, high, highs):
                cols = slice(cuts[i] * J, cuts[i + 1] * J)
                act.wait_ge(sums, i + 1)
                nc.scalar.activation(high[0:K, cols], pair_sb[0:K, 0, cols], ACT.Copy).then_inc(highs, 1)

            act.wait_ge(const_done, 1)
            nc.scalar.activation(const_sb[:, :], const_ps, ACT.Identity, bias=linb,
                                 scale=float(D)).then_inc(const_copied, 1)
            nc.scalar.activation(select_r[:, :], select_sb, ACT.Copy)
            act.wait_ge(v_multiplied, 1)
            copy_v(2, 0, VK)
            copy_v(F + 2, 0, VK)
            act.wait_ge(xa_loaded[0], 16)
            nc.scalar.activation(x_split[0:XS], x_a[0:XS, 0, :], ACT.Copy).then_inc(xa_high, 1)

            act.wait_ge(v_summed, len(V_DVE))
            copy_v(F + 2 + VK, VK, DR - F - 2)
            act.wait_ge(v_multiplied, 2)
            copy_v(2 + 3 * VK, 3 * VK, M)
            copy_v(0, M - 1, M).then_inc(v_copied, 1)
            round_high(0, 0)
            copy_d(0)
            round_high(0, 1)
            for g in range(1, 4):
                copy_d(g)
            round_high(0, 2)
            copy_d(4)
            weights_high(0, WC_CUTS, wc_sums, wc_high, wc_highs)
            copy_d(5)
            round_high(0, 3)
            copy_d(6)
            copy_d(7)
            copy_d(8)
            weights_high(1, WC_CUTS, wc_sums, wc_high, wc_highs)
            round_high(0, 4)
            weights_high(2, WC_CUTS, wc_sums, wc_high, wc_highs)
            act.wait_ge(dgroup_copied, NG)
            for m in range(5, BODY):
                if m == C:
                    act.wait_ge(z_done, C)
                    act.sem_inc(q_psum_free, 2)
                    act.sem_inc(c1_psum_free, 2)
                if m == PRODUCT_AT - LAG:
                    copy_c1(0, 0)
                for i in range(len(WQ_CUTS) - 1):
                    if WQ_AT[i] == m:
                        weights_high(i, WQ_CUTS, wq_sums, wq_high, wq_highs)
                round_high(0, m)
            with act.Fori(0, NCH // BODY - 1) as it:
                for m in range(BODY, 2 * BODY):
                    if (m - PRODUCT_AT + LAG) % C == 0:
                        copy_c1(it, (m - PRODUCT_AT + LAG) // C)
                    round_high(it, m)
            copy_c1(0, U - 1)
            act.wait_ge(total_done, 1)
            nc.scalar.activation(out_sb[:, :], out_ps, ACT.Identity, bias=const_sb[0:1, 0:1]).then_inc(out_ready, 1)

        @block.gpsimd
        def _(pool):
            nc.gpsimd.memset(ones[:, :], 1.0)
            nc.gpsimd.memset(warm_sb[:, :], 0.0).then_inc(filled, 1)
            nc.gpsimd.memset(acc[:, :], 0.0).then_inc(acc_done, 1)
            nc.gpsimd.sem_inc(z_slots_free, SLOTS)

            def weights(i, cuts, high, low, sums, highs, ready):
                cols = slice(cuts[i] * J, cuts[i + 1] * J)
                nc.gpsimd.tensor_tensor(pair_sb[0:K, 0, cols], pair_sb[0:K, 0, cols], pair_sb[0:K, 1, cols],
                                        ALU.add).then_inc(sums, 1)
                pool.wait_ge(highs, i + 1)
                nc.gpsimd.tensor_tensor(low[0:K, cols], pair_sb[0:K, 0, cols], high[0:K, cols].bitcast(fp32),
                                        ALU.subtract).then_inc(ready, 1)

            pool.wait_ge(w0_loaded, 16)
            for i in range(len(WC_CUTS) - 1):
                weights(i, WC_CUTS, wc_high, wc_low, wc_sums, wc_highs, wc_ready)
            pool.wait_ge(wc_ready, len(WC_CUTS) - 1)
            nc.gpsimd.memset(pair_sb[0:F, 1, 0:J], 0.0).then_inc(equals_cleared, 1)
            pool.wait_ge(equals_cleared, 1)
            pool.wait_ge(d_stored, 16 * DS)
            gather_d(pool, POOL_GATHERS, dpair_loaded_pool)
            for i in range(len(WQ_CUTS) - 1):
                pool.wait_ge(dpair_loaded[i], 16 * sum(g[2] == i for g in SP_GATHERS))
                pool.wait_ge(dpair_loaded_pool[i], 16 * sum(g[2] == i for g in POOL_GATHERS))
                weights(i, WQ_CUTS, wq_high, wq_low, wq_sums, wq_highs, wq_ready)

        @block.tensor
        def _(pe):
            def chunk_products(ps, high, low, m):
                c, slot = m % C, m % SLOTS
                for k, (w, z) in enumerate(((high, z_high), (low, z_high), (high, z_low))):
                    for h in range(2):
                        last = nc.tensor.matmul(ps[0:J, h * B:(h + 1) * B], w[0:K, c * J:(c + 1) * J],
                                                z[0:K, slot, h * B:(h + 1) * B],
                                                start=(c == 0 and k == 0), stop=(c == C - 1 and k == 2))
                return last

            def last_q(m, cols):
                c, slot = m % C, m % SLOTS
                for k, (w, z) in enumerate(((wq_high, z_high), (wq_low, z_high), (wq_high, z_low))):
                    last = nc.tensor.matmul(q_ps[1][0:J, cols], w[0:K, c * J:(c + 1) * J], z[0:K, slot, cols],
                                            start=False, stop=(c == C - 1 and k == 2))
                return last

            def c1_chunk(it, m):
                u, c = divmod(m, C)
                if m == 0:
                    pe.wait_ge(z_done, 3)
                if m in WC_CUTS[:-1]:
                    pe.wait_ge(wc_ready, WC_CUTS.index(m) + 1)
                pe.wait_ge(high_done, it * BODY + (m + 1))
                pe.wait_ge(low_done, it * BODY + (m + 1))
                if c == 0 and u >= 1:
                    pe.wait_ge(c1_psum_free, it * 2 + (u + 1))
                last = chunk_products(c1_ps[u % 2], wc_high, wc_low, m)
                if c == C - 1:
                    last.then_inc(c1_done, 1)

            def q_chunk(it, m):
                u, c = divmod(m, C)
                if m in WQ_CUTS[:-1]:
                    pe.wait_ge(wq_ready, WQ_CUTS.index(m) + 1)
                if c == 0:
                    pe.wait_ge(q_psum_free, it * 2 + (u + 1))
                chunk_products(q_ps[u % 2], wq_high, wq_low, m).then_inc(z_slots_free, 1)

            def select_xb(m):
                pe.wait_ge(xa_split, 1)
                for h in range(2):
                    cols = slice(h * B, (h + 1) * B)
                    last = nc.tensor.matmul(sel_ps[m][:, cols], select_r[:, T * m:T * m + 128], x_split[0:XS, cols],
                                            start=True, stop=True)
                last.then_inc(selected, 1)

            def constant():
                nc.tensor.matmul(const_ps, lw3, b2, start=True, stop=True).then_inc(const_done, 1)

            def warm():
                nc.tensor.matmul(warm_ps, warm_sb[:, 0:128], warm_sb[:, :], start=True, stop=True)

            def d_group(g):
                n = (GI if g < NG - 1 else 1) * J
                if g == 0:
                    pe.wait_ge(v_copied, 1)
                    pe.wait_ge(const_copied, 1)
                if g in W1_CUTS:
                    pe.wait_ge(w1_loaded[W1_CUTS.index(g)], 16)
                if g >= 4:
                    pe.wait_ge(dgroup_copied, g - 3)
                nc.tensor.matmul(d_ps[g % 4][0:DR, 0:n], v_sb[:, :], w1_post[0:J, g * GI * J:g * GI * J + n],
                                 start=True, stop=True).then_inc(dgroup_done, 1)

            pe.wait_ge(small_loaded, 16)
            constant()
            pe.wait_ge(filled, 1)
            for _ in range(WARM):
                warm()
            for i in V_PE:
                pe.wait_ge(w2_loaded[i], 16)
                for k in range(VK):
                    last = nc.tensor.matmul(v_ps[i][:, k:k + 1], w2_d[0:H, (i * VK + k) * H:(i * VK + k + 1) * H], lw3,
                                            start=True, stop=True)
                    if k % 2 == 0:
                        warm()
                last.then_inc(v_multiplied, 1)
            select_xb(1)
            for g in range(NG):
                d_group(g)
                if g == 1:
                    select_xb(2)
                if g == 3:
                    pe.wait_ge(z_done, 2)
                    select_xb(3)
                if g == 6:
                    pe.wait_ge(z_done, 4)
                    select_xb(4)
            c1_chunk(0, 0)
            pe.wait_ge(dgroup_copied, NG)
            select_xb(5)
            select_xb(6)
            for m in range(1, LAG):
                c1_chunk(0, m)
            whole = (NCH - LAG) // BODY
            with pe.Fori(0, whole) as it:
                for m in range(LAG, LAG + BODY):
                    q_chunk(it, m - LAG)
                    c1_chunk(it, m)
            for m in range(LAG + whole * BODY, NCH):
                q_chunk(0, m - LAG)
                c1_chunk(0, m)
            for m in range(NCH - LAG, NCH - 2):
                q_chunk(0, m)
            for h in range(2):
                last_q(NCH - 2, slice(h * B, (h + 1) * B))
                last_q(NCH - 1, slice(h * B, (h + 1) * B)).then_inc(last_q_done, 1)
            pe.wait_ge(acc_done, U + 2)
            pe.wait_ge(c1_psum_free, U + 2)
            nc.tensor.matmul(out_ps, ones[:, :], acc[:, 0:B], start=True, stop=False)
            for i in range(2):
                pe.wait_ge(last_done, i + 2)
                last = nc.tensor.matmul(out_ps[:, i * B // 2:(i + 1) * B // 2], ones[:, :],
                                        prod[:, B + i * B // 2:B + (i + 1) * B // 2], start=False, stop=(i == 1))
            last.then_inc(total_done, 1)


def kernel(r_inputs, L0_rec_W0, L0_rec_W1, L0_rec_W2, L0_rec_b0, L0_rec_b1, L0_rec_b2, L0_rec_lin_w, L0_rec_lin_b):
    import numpy as np
    import concourse.bacc as bacc
    from concourse.bass_utils import run_bass_kernel_spmd

    x, w0, w1, w2, b0, b1, b2, lw, lb = (np.asarray(a) for a in (
        r_inputs, L0_rec_W0, L0_rec_W1, L0_rec_W2, L0_rec_b0, L0_rec_b1, L0_rec_b2, L0_rec_lin_w, L0_rec_lin_b))
    f = x.dtype
    xt = np.ones((F, D * B), f)
    xt[:M] = x.transpose(1, 2, 0).reshape(M, D * B)
    p = np.arange(128)
    xa = np.ascontiguousarray(xt[(p % F - p // F) % F])
    xw = np.ascontiguousarray(xt[np.arange(SW) % F])
    full = np.zeros((F, F, J), f)
    full[:M, :M, :H] = w0
    full[M, M, :H] = b0
    full[M, M, H] = 1
    rows = np.arange(K)
    a = (rows % F - rows // F) % F
    w0_pairs = np.zeros((128, 2, C, J), f)
    for c in range(C):
        b = (rows + T * c) % F
        w0_pairs[:K, 0, c] = full[a, b]
        w0_pairs[:K, 1, c] = full[b, a]
    w0_pairs[:F, 1, 0] = 0
    w1x = np.zeros((112, F, J), f)
    w1x[:H, :M, :H] = w1.transpose(2, 0, 1)
    w1x[:H, M, H] = b1
    w1x[H, M, :H] = lw[:H, 0]
    w2h = np.zeros((112, M, H), f)
    w2h[:H] = w2.transpose(1, 0, 2)
    for i in V_PE:
        w2h[:H, i * VK:(i + 1) * VK] = w2[i * VK:(i + 1) * VK].transpose(2, 0, 1)
    small = np.zeros((112, SMALL), f)
    small[:H, [1, F + 1]] = lw[H:2 * H]
    small[H, [1, F + 1]] = 1
    small[:H, DR:DR + H] = lw[2 * H:, 0]
    small[:H, DR + H] = lw[2 * H:, 0]
    small[:H, DR + H + 1] = b2
    small[0, DR + H + 2] = lb[0]
    feature = (p % F - p // F) % F
    for first, n in ((0, F), (LOW_AT, 2 * F - LOW_AT), (2 * F + 1, XS - 2 * F - 1)):
        small[first:first + n, DR + H + 3:] = feature[first:first + n, None] == np.arange(SW) % F
    arrays = {
        "xa": xa, "xw": xw, "w0_pairs": w0_pairs.reshape(128, 2, C * J), "w1x": w1x.reshape(112, F * J),
        "w2h": w2h.reshape(112, M * H), "small": small,
    }
    nc = bacc.Bacc("TRN2", target_bir_lowering=False, num_devices=1)
    args = {n: nc.dram_tensor(n, v.shape, mybir.dt.from_np(v.dtype), kind="ExternalInput").ap()
            for n, v in arrays.items()}
    out = nc.dram_tensor("out", (1, B), mybir.dt.float32, kind="ExternalOutput").ap()
    build(nc, out=out, **args)
    r = run_bass_kernel_spmd(nc, [arrays], core_ids=[0])
    return r.results[0]["out"].reshape(B, 1)
```
